# Optimizing a Trainium2 kernel written in Bass

```python
import numpy as np
import jax
import jax.numpy as jnp

def _softmax(x, axis=-1):
    return jax.nn.softmax(x, axis=axis)

def _gelu(x):
    return jax.nn.gelu(x, approximate=True)

def _silu(x):
    return jax.nn.silu(x)

def _sigmoid(x):
    return jax.nn.sigmoid(x)

def _layernorm(x, axis=-1, eps=1e-05):
    m = jnp.mean(x, axis=axis, keepdims=True)
    v = jnp.var(x, axis=axis, keepdims=True)
    return (x - m) / jnp.sqrt(v + eps)

def _scatter_add(tgt, idx, src, axis=0):
    return tgt.at[idx].add(src)

def _segment_sum(src, seg, n):
    return jax.ops.segment_sum(src, seg, n)
kernel_name = 'mk_gnn_ffn_d1_gnn_r32_cb6c92'

def setup_inputs(seed: int=0):
    np.random.seed(seed)
    _w = jnp.asarray

    def _rec_inputs():
        import jax
        import jax.numpy as jnp
        _gk = jax.random.key(seed)
        x = -0.0003713 + 1 * jax.random.normal(jax.random.fold_in(_gk, 1), (3125, 256), jnp.float32)
        src = jax.random.randint(jax.random.fold_in(_gk, 2), (50000,), 0, 3125, jnp.int32)
        dst = jnp.minimum((3125 * jax.random.uniform(jax.random.fold_in(_gk, 3), (50000,)) ** 2.0).astype(jnp.int32), 99999)
        _o = jnp.argsort(dst, stable=True)
        src = src[_o]
        dst = dst[_o]
        edge_attr_64 = 0.000189758 + 1.00013 * jax.random.normal(jax.random.fold_in(_gk, 11), (50000, 64), jnp.float32)
        return (x, src, dst, edge_attr_64)
    x, src, dst, edge_attr_64 = _rec_inputs()

    def _L0_gnn_setup():
        import jax, jax.numpy as jnp
        import numpy as np
        N, E = (50000, 25000)
        HID, EDIM, HEADS = (256, 64, 8)
        C = HID // HEADS
        NEG_SLOPE = 0.2
        LN_EPS = 1e-05

        def _gat_block(x, edge_index, edge_attr, W, W_e, att_src, att_dst, att_edge, bias, gamma, beta):
            n = x.shape[0]
            src, dst = (edge_index[0], edge_index[1])
            xp = (x @ W).reshape(n, HEADS, C)
            a_src = jnp.einsum('nhc,hc->nh', xp, att_src)
            a_dst = jnp.einsum('nhc,hc->nh', xp, att_dst)
            ep = (edge_attr @ W_e).reshape(-1, HEADS, C)
            a_edge = jnp.einsum('ehc,hc->eh', ep, att_edge)
            alpha = a_src[src] + a_dst[dst] + a_edge
            alpha = jax.nn.leaky_relu(alpha, NEG_SLOPE)
            m = jax.ops.segment_max(alpha, dst, num_segments=n)
            m = jnp.where(jnp.isfinite(m), m, 0.0)
            ea = jnp.exp(alpha - m[dst])
            den = jax.ops.segment_sum(ea, dst, num_segments=n)
            attn = ea / (den[dst] + 1e-16)
            msg = xp[src] * attn[:, :, None]
            out = jax.ops.segment_sum(msg, dst, num_segments=n)
            h = out.reshape(n, HEADS * C) + bias
            y = x + h
            mu = jnp.mean(y, axis=-1, keepdims=True)
            var = jnp.var(y, axis=-1, keepdims=True)
            return (y - mu) * jax.lax.rsqrt(var + LN_EPS) * gamma + beta
        key = jax.random.key(seed)
        ks = jax.random.split(key, 12)
        s = 1.0 / np.sqrt(HID)
        se = 1.0 / np.sqrt(EDIM)
        return {'x': jax.random.normal(ks[0], (N, HID), jnp.float32), 'edge_index': jax.random.randint(ks[1], (2, E), 0, N, jnp.int32), 'edge_attr': jax.random.normal(ks[2], (E, EDIM), jnp.float32), 'W': jax.random.uniform(ks[3], (HID, HEADS * C), jnp.float32, -s, s), 'W_e': jax.random.uniform(ks[4], (EDIM, HEADS * C), jnp.float32, -se, se), 'att_src': jax.random.normal(ks[5], (HEADS, C), jnp.float32) * 0.1, 'att_dst': jax.random.normal(ks[6], (HEADS, C), jnp.float32) * 0.1, 'att_edge': jax.random.normal(ks[7], (HEADS, C), jnp.float32) * 0.1, 'bias': jnp.zeros((HEADS * C,), jnp.float32), 'gamma': jnp.ones((HID,), jnp.float32), 'beta': jnp.zeros((HID,), jnp.float32)}
    _L0_gnn_all = _L0_gnn_setup()
    _L0_gnn_in = {k: v for k, v in _L0_gnn_all.items() if k in ('W', 'W_e', 'att_src', 'att_dst', 'att_edge', 'bias', 'gamma', 'beta')}
    del _L0_gnn_all

    def _L0_ffn_setup():
        import jax, jax.numpy as jnp
        import numpy as np
        TOP_K = 2
        key = jax.random.key(seed)
        ks = jax.random.split(key, 4)
        B, L, D, H, E = (8, 128, 256, 1024, 8)
        s = 0.02
        return {'x': jax.random.normal(ks[0], (B, L, D), jnp.float32), 'Wg': jax.random.normal(ks[1], (D, E), jnp.float32) * s, 'bg': jnp.zeros((E,), jnp.float32), 'W1': jax.random.normal(ks[2], (E, D, H), jnp.float32) * s, 'b1': jnp.zeros((E, H), jnp.float32), 'W2': jax.random.normal(ks[3], (E, H, D), jnp.float32) * s, 'b2': jnp.zeros((E, D), jnp.float32)}
    _L0_ffn_all = _L0_ffn_setup()
    _L0_ffn_in = {k: v for k, v in _L0_ffn_all.items() if k in ('Wg', 'bg', 'W1', 'b1', 'W2', 'b2')}
    del _L0_ffn_all
    return {'x': x, 'src': src, 'dst': dst, 'edge_attr_64': edge_attr_64, 'L0_gnn_W': _L0_gnn_in['W'], 'L0_gnn_W_e': _L0_gnn_in['W_e'], 'L0_gnn_att_src': _L0_gnn_in['att_src'], 'L0_gnn_att_dst': _L0_gnn_in['att_dst'], 'L0_gnn_att_edge': _L0_gnn_in['att_edge'], 'L0_gnn_bias': _L0_gnn_in['bias'], 'L0_gnn_gamma': _L0_gnn_in['gamma'], 'L0_gnn_beta': _L0_gnn_in['beta'], 'L0_ffn_Wg': _L0_ffn_in['Wg'], 'L0_ffn_bg': _L0_ffn_in['bg'], 'L0_ffn_W1': _L0_ffn_in['W1'], 'L0_ffn_b1': _L0_ffn_in['b1'], 'L0_ffn_W2': _L0_ffn_in['W2'], 'L0_ffn_b2': _L0_ffn_in['b2']}

def reference(x, src, dst, edge_attr_64, L0_gnn_W, L0_gnn_W_e, L0_gnn_att_src, L0_gnn_att_dst, L0_gnn_att_edge, L0_gnn_bias, L0_gnn_gamma, L0_gnn_beta, L0_ffn_Wg, L0_ffn_bg, L0_ffn_W1, L0_ffn_b1, L0_ffn_W2, L0_ffn_b2):
    import jax
    import jax.numpy as jnp

    def _L0_gnn_ref(x, edge_index, edge_attr, W, W_e, att_src, att_dst, att_edge, bias, gamma, beta):
        import jax, jax.numpy as jnp
        import numpy as np
        N, E = (50000, 25000)
        HID, EDIM, HEADS = (256, 64, 8)
        C = HID // HEADS
        NEG_SLOPE = 0.2
        LN_EPS = 1e-05

        def _gat_block(x, edge_index, edge_attr, W, W_e, att_src, att_dst, att_edge, bias, gamma, beta):
            n = x.shape[0]
            src, dst = (edge_index[0], edge_index[1])
            xp = (x @ W).reshape(n, HEADS, C)
            a_src = jnp.einsum('nhc,hc->nh', xp, att_src)
            a_dst = jnp.einsum('nhc,hc->nh', xp, att_dst)
            ep = (edge_attr @ W_e).reshape(-1, HEADS, C)
            a_edge = jnp.einsum('ehc,hc->eh', ep, att_edge)
            alpha = a_src[src] + a_dst[dst] + a_edge
            alpha = jax.nn.leaky_relu(alpha, NEG_SLOPE)
            m = jax.ops.segment_max(alpha, dst, num_segments=n)
            m = jnp.where(jnp.isfinite(m), m, 0.0)
            ea = jnp.exp(alpha - m[dst])
            den = jax.ops.segment_sum(ea, dst, num_segments=n)
            attn = ea / (den[dst] + 1e-16)
            msg = xp[src] * attn[:, :, None]
            out = jax.ops.segment_sum(msg, dst, num_segments=n)
            h = out.reshape(n, HEADS * C) + bias
            y = x + h
            mu = jnp.mean(y, axis=-1, keepdims=True)
            var = jnp.var(y, axis=-1, keepdims=True)
            return (y - mu) * jax.lax.rsqrt(var + LN_EPS) * gamma + beta
        return _gat_block(x, edge_index, edge_attr, W, W_e, att_src, att_dst, att_edge, bias, gamma, beta)

    def _L0_ffn_ref(x, Wg, bg, W1, b1, W2, b2):
        import jax, jax.numpy as jnp
        import numpy as np
        TOP_K = 2
        B, L, D = x.shape
        E = W1.shape[0]
        xf = x.reshape(-1, D)
        gate_logits = xf @ Wg + bg
        top_w, top_i = jax.lax.top_k(gate_logits, TOP_K)
        top_w = jax.nn.softmax(top_w, axis=-1)
        w_dense = jnp.sum(jax.nn.one_hot(top_i, E, dtype=xf.dtype) * top_w[..., None], axis=1)
        out = jnp.zeros_like(xf)
        for e in range(E):
            h = jax.nn.gelu(xf @ W1[e] + b1[e], approximate=False)
            out = out + w_dense[:, e:e + 1] * (h @ W2[e] + b2[e])
        return out.reshape(B, L, D)
    edge_index = jnp.stack([src, dst])
    x = x + _L0_gnn_ref(_layernorm(x, axis=-1), edge_index, edge_attr_64, L0_gnn_W, L0_gnn_W_e, L0_gnn_att_src, L0_gnn_att_dst, L0_gnn_att_edge, L0_gnn_bias, L0_gnn_gamma, L0_gnn_beta)
    x = x + _L0_ffn_ref(_layernorm(x, axis=-1)[None], L0_ffn_Wg, L0_ffn_bg, L0_ffn_W1, L0_ffn_b1, L0_ffn_W2, L0_ffn_b2)[0]
    return x

_drawn_inputs = setup_inputs


def setup_inputs(seed=0):
    import zlib

    import numpy as np

    out = dict(_drawn_inputs(seed))
    spreads = {'L0_gnn_bias': (0.0, 0.1),
     'L0_gnn_gamma': (1.0, 0.2),
     'L0_gnn_beta': (0.0, 0.1),
     'L0_ffn_bg': (0.0, 0.316),
     'L0_ffn_b1': (0.0, 0.6),
     'L0_ffn_b2': (0.0, 0.1)}
    factors = {'L0_gnn_att_dst': 5.76}
    for name, (base, spread) in spreads.items():
        noise = np.random.default_rng([zlib.crc32(name.encode()), seed]).standard_normal(out[name].shape)
        drawn = base * np.exp(spread * noise) if base else spread * noise
        out[name] = jnp.asarray(drawn.astype(out[name].dtype))
    for name, factor in factors.items():
        out[name] = (out[name] * factor).astype(out[name].dtype)
    return out
```

```python
import concourse.bass as bass
from concourse import mybir
from contextlib import ExitStack

F32 = mybir.dt.float32
BF16 = mybir.dt.bfloat16
I32 = mybir.dt.int32
U32 = mybir.dt.uint32
ALU = mybir.AluOpType
ACT = mybir.ActivationFunctionType
AX = mybir.AxisListType

P = 128
BIG = 1.0e30
DMA = 16


class Step:

    def __init__(self, j, off):
        self.j, self.off, self.slot = j, off, off % 2

    def times(self, k, plus=0):
        return k * self.off + plus if self.j is None else self.j * (2 * k) + (k * self.off + plus)

    def uses(self, k):
        n = self.off // 2 + 1
        return k * n if self.j is None else self.j * k + k * n

    def next(self):
        return Step(self.j, self.off + 1)


class Counts:

    def __init__(self, sem, **names):
        self.names = {engine: text.split() for engine, text in names.items()}
        self.sems = {name: sem(name) for text in self.names.values() for name in text}

    def __getitem__(self, name):
        return self.sems[name]

    def start(self, engine, which):
        for name in self.names[which]:
            engine.sem_inc(self.sems[name], 1)

    def wait(self, engine, name, value):
        engine.wait_ge(self.sems[name], value + 1)


def two_step_loop(engine, steps, body):
    with engine.Fori(0, steps // 2) as j:
        body(Step(j, 0))
        body(Step(j, 1))
    if steps % 2:
        body(Step(None, steps - 1))


def build(nc, x, edges, edge_attr, W, W_e, att_src, att_dst, att_edge, g_bias, g_gamma, g_beta,
          Wg, bg, W1, b1, W2, b2, out):
    N, D = x.shape
    E, EDIM = edge_attr.shape
    HEADS, C = att_src.shape
    NX, _, HID = W1.shape
    KD = D // P
    KH = HID // P
    NT = -(-N // P)
    LAST = N - (NT - 1) * P
    CW = C + 1
    TW = HEADS * CW
    G = 16
    GROUPS = -(-((E - 1) // P + 1 + NT) // G)
    TILES = GROUPS * G
    GT = TILES + G
    GH = G * HEADS
    XS = (2 * N + NX * (P - 1)) // P
    EPS = 1e-5
    SLOPE = 0.2
    assert GH == P and N > (NT - 1) * P and XS % 2 == 0

    table = nc.dram_tensor("node_table", (N, TW), F32).ap()
    slots_in = nc.dram_tensor("slots_in", ((XS + 2) * P, D), F32).ap()
    slots_out = nc.dram_tensor("slots_out", (XS * P, D), F32).ap()

    top = ExitStack()

    def sb(name, shape, dt=F32, stack=None):
        return (stack or top).enter_context(nc.sbuf_tensor(name, shape, dt))

    def pb(name, shape, dt=F32, stack=None):
        return (stack or top).enter_context(nc.psum_tensor(name, shape, dt))

    def sem(name, stack=None):
        return (stack or top).enter_context(nc.semaphore(name))

    with top:
        X = sb("X", [P, NT, D])
        XN = sb("XN", [P, NT, D])
        acc = sb("acc", [P, NT * TW])
        acc_v = acc[:, :].rearrange("p (t h c) -> p t h c", t=NT, c=CW)
        ident = sb("ident", [P, P])
        before = sb("before", [P, P])
        ones = sb("ones", [P, P])
        identb = sb("identb", [P, P], BF16)
        iota_row = sb("iota_row", [P, P])
        iota_p = sb("iota_p", [P, 1])
        stats = sb("stats", [P, NT, 6])
        mv = sb("mv", [P, NT, 2])
        rstd = sb("rstd", [P, NT])
        eps = sb("eps", [P, 1])
        wbuf = sb("wbuf", [P, 2, KD * HID + KH * D])
        expert_w = [sem(f"expert_w{i}") for i in range(2)]
        zeros_out = sem("zeros_out")

        def load_expert(eng, e, slot):
            eng.dma_start(wbuf[:, slot, 0:KD * HID].rearrange("p (k n) -> p k n", k=KD),
                          W1[e].rearrange("(k p) n -> p k n", p=P)).then_inc(expert_w[slot], DMA)
            eng.dma_start(wbuf[:, slot, KD * HID:].rearrange("p (k n) -> p k n", k=KH),
                          W2[e].rearrange("(k p) n -> p k n", p=P)).then_inc(expert_w[slot], DMA)

        graph = ExitStack()
        with graph:
            gs = lambda name, shape, dt=F32: sb(name, shape, dt, graph)
            AD = gs("AD", [P, NT * HEADS])
            AD3 = gs("AD3", [P, 3, NT * HEADS], BF16)
            geo = gs("geo", [P, GT])
            penb = gs("penb", [P, GT + 1])
            edge_row = gs("edge_row", [1, GT], I32)
            ad_off = gs("ad_off", [1, GT], I32)
            acc_off = gs("acc_off", [1, GT], I32)
            We8 = gs("We8", [P, P // EDIM, HEADS])

            prep = ExitStack()
            with prep:
                ps = lambda name, shape, dt=F32: sb(name, shape, dt, prep)
                Wx = ps("Wx", [P, KD, TW + HEADS])
                Wx_h = Wx[:, :, 0:TW].rearrange("p k (h c) -> p k h c", c=CW)
                attb = ps("attb", [P, 3, D])
                We = ps("We", [P, D])
                fold = ps("fold", [P, 3, KD, D])
                XT = ps("XT", [P, 2, KD, P])
                TB = ps("TB", [P, 2, TW])
                dsti = ps("dsti", [E // 400, 400], I32)
                dstf = ps("dstf", [E // 400, 400])
                below = ps("below", [E // 400, 400])
                cnt = ps("cnt", [E // 400, NT + 1])
                col = ps("col", [NT, 16])
                coli = ps("coli", [NT, 2], I32)
                iota_t = ps("iota_t", [P, GT])
                mask1 = ps("mask1", [NT, GT])
                mask = ps("mask", [NT, GT])
                spread = ps("spread", [NT, 2, P])
                first = ps("first", [P, GT])
                firstc = ps("firstc", [P, GT])
                bin128 = ps("bin128", [P, GT])
                zeros = ps("zeros", [P, 2048])
                pX = [pb(f"pX{i}", [P, 512], F32, prep) for i in range(2)]
                pY = [pb(f"pY{i}", [P, 512], F32, prep) for i in range(2)]
                pG = [pb(f"pG{i}", [P, 512], F32, prep) for i in range(2)]
                x_in = sem("x_in", prep)
                w_in = sem("w_in", prep)
                dst_in = sem("dst_in", prep)
                consts = sem("consts", prep)
                dve_order = sem("dve_order", prep)
                pool_order = sem("pool_order", prep)
                var_done = sem("var_done", prep)
                std_done = sem("std_done", prep)
                xn_done = sem("xn_done", prep)
                folded = sem("folded", prep)
                xt_turned = sem("xt_turned", prep)
                xt_copied = sem("xt_copied", prep)
                xp_done = sem("xp_done", prep)
                xp_copied = sem("xp_copied", prep)
                table_out = [sem(f"table_out{i}", prep) for i in range(2)]
                counts_done = sem("counts_done", prep)
                bins_summed = sem("bins_summed", prep)
                tiles_in = sem("tiles_in", prep)
                bins_ordered = sem("bins_ordered", prep)
                masks_done = sem("masks_done", prep)
                geo_done = sem("geo_done", prep)
                zero_set = sem("zero_set", prep)

                with nc.Block() as block:
                    @block.sync
                    def _(sp):
                        sp.dma_start(dsti[:, :], edges[1, :].rearrange("(p f) -> p f", f=400)).then_inc(dst_in, DMA)
                        sp.wait_ge(consts, 1)
                        sp.dma_start(X[:, 0:NT - 1, :], x[0:(NT - 1) * P, :].rearrange("(t p) d -> p t d", p=P)
                                     ).then_inc(x_in, DMA)
                        sp.dma_start(X[0:LAST, NT - 1, :], x[(NT - 1) * P:N, :]).then_inc(x_in, DMA)
                        for k in range(KD):
                            sp.dma_start(Wx_h[:, k, :, 0:C],
                                         W[k * P:(k + 1) * P, :].rearrange("p (h c) -> p h c", c=C)
                                         ).then_inc(w_in, DMA)
                        for i in range(P // EDIM):
                            sp.dma_start(We[i * EDIM:(i + 1) * EDIM, :], W_e).then_inc(w_in, DMA)
                        for i, a in enumerate((att_src, att_dst, att_edge)):
                            sp.dma_start(attb[:, i, :], a.rearrange("h c -> (h c)").partition_broadcast(P)
                                         ).then_inc(w_in, DMA)
                        for t in range(NT):
                            rows = P if t < NT - 1 else LAST
                            sp.wait_ge(xp_copied, t + 1)
                            sp.dma_start(table[t * P:t * P + rows, :], TB[0:rows, t % 2, :]
                                         ).then_inc(table_out[t % 2], DMA)
                        for i in range(2):
                            sp.wait_ge(table_out[i], len(range(i, NT, 2)) * DMA)
                        sp.wait_ge(zero_set, 1)
                        flat = slots_in.rearrange("(g p) d -> g p d", p=P)
                        for g in range(0, XS + 2, 8):
                            n = min(8, XS + 2 - g)
                            sp.dma_start(flat[g:g + n].rearrange("g p d -> p g d"),
                                         zeros[:, 0:n * D].rearrange("p (g d) -> p g d", d=D)
                                         ).then_inc(zeros_out, DMA)
                        sp.wait_ge(zeros_out, -(-(XS + 2) // 8) * DMA)

                    @block.gpsimd
                    def _(pool):
                        nc.gpsimd.memset(X[:, NT - 1, :], 0.0).then_inc(consts, 1)
                        nc.gpsimd.memset(ident[:, :], 0.0)
                        nc.gpsimd.memset(before[:, :], 1.0)
                        nc.gpsimd.memset(ones[:, :], 1.0)
                        nc.gpsimd.memset(eps[:, :], EPS)
                        nc.gpsimd.memset(col[:, :], 0.0)
                        nc.gpsimd.iota(iota_row[:, :], pattern=[[1, P]], base=0, channel_multiplier=0,
                                       allow_small_or_imprecise_dtypes=True)
                        nc.gpsimd.iota(iota_t[:, :], pattern=[[1, GT]], base=0, channel_multiplier=0,
                                       allow_small_or_imprecise_dtypes=True)
                        nc.gpsimd.iota(iota_p[:, :], pattern=[[0, 1]], base=0, channel_multiplier=1,
                                       allow_small_or_imprecise_dtypes=True).then_inc(pool_order, 1)
                        pool.wait_ge(pool_order, 1)
                        nc.gpsimd.affine_select(out=ident[:, :], in_=ident[:, :], compare_op=ALU.not_equal, fill=1.0,
                                                base=0, pattern=[[-1, P]], channel_multiplier=1).then_inc(consts, 1)
                        nc.gpsimd.affine_select(out=before[:, :], in_=before[:, :], compare_op=ALU.is_gt, fill=0.0,
                                                base=0, pattern=[[1, P]], channel_multiplier=-1).then_inc(consts, 1)
                        nc.gpsimd.memset(zeros[:, :], 0.0).then_inc(zero_set, 1)
                        nc.gpsimd.memset(acc[:, :], 0.0)
                        for e in range(2):
                            load_expert(pool, e, e)

                    @block.vector
                    def _(dve):
                        n = [0]

                        def link(ins):
                            n[0] += 1
                            ins.then_inc(dve_order, 1)
                            dve.wait_ge(dve_order, n[0])

                        dve.wait_ge(dst_in, DMA)
                        link(nc.vector.tensor_copy(dstf[:, :], dsti[:, :]))
                        for b in range(NT + 1):
                            link(nc.vector.tensor_scalar(below[:, :], dstf[:, :], float(P * b), None, ALU.is_lt,
                                                         ALU.add, accum_out=cnt[:, b:b + 1]))
                        dve.sem_inc(counts_done, 1)
                        dve.wait_ge(x_in, 2 * DMA)
                        for t in range(NT):
                            nc.vector.bn_stats(stats[:, t, :], X[:, t, :]).then_inc(dve_order, 1)
                        n[0] += NT
                        dve.wait_ge(dve_order, n[0])
                        for t in range(NT):
                            last = nc.vector.bn_aggr(mv[:, t, :], stats[:, t, :])
                        last.then_inc(var_done, 1)
                        dve.wait_ge(w_in, (2 + P // EDIM + 3) * DMA)
                        for k in range(KD):
                            for i in range(2):
                                link(nc.vector.tensor_tensor(
                                    fold[:, i, k, :].rearrange("p (h c) -> p h c", c=C), Wx_h[:, k, :, 0:C],
                                    attb[:, i, :].rearrange("p (h c) -> p h c", c=C), ALU.mult))
                                dst = Wx_h[:, k, :, C] if i == 0 else Wx[:, k, TW:TW + HEADS]
                                link(nc.vector.tensor_reduce(dst, fold[:, i, k, :].rearrange("p (h c) -> p h c", c=C),
                                                             axis=AX.X, op=ALU.add))
                        link(nc.vector.tensor_tensor(fold[:, 2, 0, :], We[:, :], attb[:, 2, :], ALU.mult))
                        link(nc.vector.memset(We8[:, :, :], 0.0))
                        for i in range(P // EDIM):
                            half = slice(i * EDIM, (i + 1) * EDIM)
                            link(nc.vector.tensor_reduce(We8[half, i, :], fold[half, 2, 0, :].rearrange("p (h c) -> p h c", c=C),
                                                         axis=AX.X, op=ALU.add))
                        dve.sem_inc(folded, 1)
                        dve.wait_ge(std_done, 1)
                        link(nc.vector.reciprocal(rstd[:, :], rstd[:, :]))
                        for t in range(NT):
                            nc.vector.tensor_scalar(XN[:, t, :], X[:, t, :], mv[:, t, 0:1], rstd[:, t:t + 1],
                                                    ALU.subtract, ALU.mult).then_inc(xn_done, 1)
                        dve.wait_ge(bins_summed, 1)
                        link(nc.vector.tensor_copy(col[:, 0:2], pG[0][0:NT, 0:2]))
                        link(nc.vector.tensor_tensor(col[:, 2:3], col[:, 1:2], col[:, 0:1], ALU.subtract))
                        link(nc.vector.tensor_scalar_add(coli[:, 0:1], col[:, 2:3], float(P - 1)))
                        link(nc.vector.tensor_single_scalar(coli[:, 1:2], coli[:, 0:1], 7, ALU.arith_shift_right))
                        link(nc.vector.tensor_scalar_max(col[:, 3:4], coli[:, 1:2], 1.0))
                        dve.sem_inc(tiles_in, 1)
                        dve.wait_ge(bins_ordered, 1)
                        link(nc.vector.tensor_copy(col[:, 4:5], pG[1][0:NT, 0:1]))
                        link(nc.vector.tensor_tensor(col[:, 5:6], col[:, 4:5], col[:, 3:4], ALU.add))
                        link(nc.vector.tensor_scalar(col[:, 7:8], iota_p[0:NT, :], float(NT - 1), float(2 * GT),
                                                     ALU.is_ge, ALU.mult))
                        link(nc.vector.tensor_tensor(col[:, 5:6], col[:, 5:6], col[:, 7:8], ALU.add))
                        link(nc.vector.scalar_tensor_tensor(col[:, 6:7], col[:, 4:5], float(-P), col[:, 0:1],
                                                            ALU.mult, ALU.add))
                        link(nc.vector.tensor_scalar(mask1[:, :], iota_t[0:NT, :], col[:, 4:5], None, ALU.is_ge))
                        link(nc.vector.scalar_tensor_tensor(mask[:, :], iota_t[0:NT, :], col[:, 5:6], mask1[:, :],
                                                            ALU.is_lt, ALU.mult))
                        link(nc.vector.tensor_scalar(spread[:, 0, :], ones[0:NT, :], col[:, 6:7], None, ALU.mult))
                        link(nc.vector.tensor_scalar(spread[:, 1, :], ones[0:NT, :], iota_p[0:NT, :], float(P),
                                                     ALU.mult, ALU.mult))
                        dve.sem_inc(masks_done, 1)
                        link(nc.vector.tensor_copy(identb[:, :], ident[:, :]))
                        dve.wait_ge(xp_copied, NT)
                        link(nc.vector.tensor_copy(AD3[:, 0, :], AD[:, :]))
                        link(nc.vector.tensor_tensor(AD[:, :], AD[:, :], AD3[:, 0, :], ALU.subtract))
                        link(nc.vector.tensor_copy(AD3[:, 1, :], AD[:, :]))
                        link(nc.vector.tensor_tensor(AD3[:, 2, :], AD[:, :], AD3[:, 1, :], ALU.subtract))
                        dve.wait_ge(geo_done, 1)
                        link(nc.vector.scalar_tensor_tensor(first[:, :], iota_t[:, :], float(P), pG[0][:, 0:GT],
                                                            ALU.mult, ALU.add))
                        link(nc.vector.tensor_copy(bin128[:, :], pG[1][:, 0:GT]))
                        link(nc.vector.tensor_scalar_min(firstc[:, :], first[:, :], float(E - P)))
                        link(nc.vector.tensor_copy(edge_row[:, :], firstc[0:1, :]))
                        link(nc.vector.tensor_scalar_mul(ad_off[:, :], bin128[0:1, :], HEADS / P))
                        link(nc.vector.tensor_scalar_mul(acc_off[:, :], bin128[0:1, :], TW / P))
                        link(nc.vector.tensor_tensor(first[:, :], first[:, :], firstc[:, :], ALU.subtract))
                        link(nc.vector.tensor_scalar(first[:, :], first[:, :], iota_p[:, :], -8192.0,
                                                     ALU.is_gt, ALU.mult))
                        link(nc.vector.tensor_tensor(geo[:, :], bin128[:, :], first[:, :], ALU.add))
                        link(nc.vector.memset(penb[:, :], -BIG))
                        link(nc.vector.tensor_tensor(first[:, 1:GT], bin128[:, 1:GT], bin128[:, 0:GT - 1],
                                                     ALU.subtract))
                        link(nc.vector.tensor_scalar(penb[:, 1:GT], first[:, 1:GT], 0.0, -BIG,
                                                     ALU.not_equal, ALU.mult))

                    @block.scalar
                    def _(act):
                        act.wait_ge(consts, 3)
                        act.wait_ge(var_done, 1)
                        nc.scalar.activation(rstd[:, :], mv[:, :, 1], ACT.Sqrt, bias=eps[:, :]).then_inc(std_done, 1)
                        for t in range(NT):
                            act.wait_ge(xt_turned, t + 1)
                            if t >= 2:
                                act.wait_ge(xp_done, t - 1)
                            nc.scalar.copy(XT[:, t % 2, :, :], pX[t % 2][:, 0:KD * P].rearrange("p (k n) -> p k n", k=KD)
                                           ).then_inc(xt_copied, 1)
                            act.wait_ge(xp_done, t + 1)
                            if t >= 2:
                                act.wait_ge(table_out[t % 2], t // 2 * DMA)
                            nc.scalar.copy(AD[:, t * HEADS:(t + 1) * HEADS], pY[t % 2][:, TW:TW + HEADS])
                            nc.scalar.copy(TB[:, t % 2, :], pY[t % 2][:, 0:TW]).then_inc(xp_copied, 1)

                    @block.tensor
                    def _(pe):
                        pe.wait_ge(consts, 3)
                        pe.wait_ge(counts_done, 1)
                        B = E // 400
                        nc.tensor.matmul(pG[0][0:NT, 0:1], cnt[:, 0:NT], ones[0:B, 0:1], start=True, stop=True)
                        nc.tensor.matmul(pG[0][0:NT, 1:2], cnt[:, 1:NT + 1], ones[0:B, 0:1], start=True, stop=True
                                         ).then_inc(bins_summed, 1)
                        pe.wait_ge(folded, 1)
                        for t in range(NT):
                            pe.wait_ge(xn_done, t + 1)
                            for k in range(KD):
                                last = nc.tensor.transpose(pX[t % 2][:, k * P:(k + 1) * P],
                                                           XN[:, t, k * P:(k + 1) * P], ident[:, :])
                            last.then_inc(xt_turned, 1)
                            pe.wait_ge(xt_copied, t + 1)
                            if t >= 2:
                                pe.wait_ge(xp_copied, t - 1)
                            for k in range(KD):
                                last = nc.tensor.matmul(pY[t % 2][:, 0:TW + HEADS], XT[:, t % 2, k, :], Wx[:, k, :],
                                                        start=(k == 0), stop=(k == KD - 1))
                            last.then_inc(xp_done, 1)
                        pe.wait_ge(tiles_in, 1)
                        nc.tensor.matmul(pG[1][0:NT, 0:1], before[0:NT, 0:NT], col[:, 3:4], start=True, stop=True
                                         ).then_inc(bins_ordered, 1)
                        pe.wait_ge(masks_done, 1)
                        nc.tensor.matmul(pG[0][:, 0:GT], spread[:, 0, :], mask[:, :], start=True, stop=True)
                        nc.tensor.matmul(pG[1][:, 0:GT], spread[:, 1, :], mask[:, :], start=True, stop=True
                                         ).then_inc(geo_done, 1)

            edge = ExitStack()
            with edge:
                es = lambda name, shape, dt=F32: sb(name, shape, dt, edge)
                two = range(2)
                SDi = [es(f"SDi{i}", [2 * G, P], I32) for i in two]
                SDf = es("SDf", [P, P])
                AT = es("AT", [P, G, EDIM])
                ATT = es("ATT", [P, G // 2, P])
                srcI = [es(f"srcI{i}", [P, G], I32) for i in two]
                dloc = es("dloc", [P, G])
                dst8 = es("dst8", [P, G, HEADS])
                OH = es("OH", [P, G, P])
                OHb = [es(f"OHb{i}", [P, G, P], BF16) for i in two]
                OHT = [es(f"OHT{i}", [P, G, P], BF16) for i in two]
                gath = [es(f"gath{i}", [P, G, TW]) for i in two]
                dT = es("dT", [P, P])
                step_ = es("step_", [P, P])
                seg_end = [es(f"seg_end{i}", [P, P]) for i in two]
                seg_pen = [es(f"seg_pen{i}", [P, P]) for i in two]
                al0 = es("al0", [P, G, HEADS])
                al = es("al", [P, G, HEADS])
                run = es("run", [P, P])
                runend = es("runend", [P, P])
                endp = es("endp", [P, 4, G, HEADS], BF16)
                rest = es("rest", [P, GH])
                absent = es("absent", [P, G, HEADS])
                penF = [es(f"penF{i}", [P, HEADS, G + 1]) for i in two]
                penR = [es(f"penR{i}", [P, HEADS, G]) for i in two]
                mF = es("mF", [P, HEADS, G + 1])
                mR = es("mR", [P, HEADS, G])
                F = es("F", [P, HEADS, G + 1])
                R = es("R", [P, HEADS, G])
                M = es("M", [P, HEADS, G])
                Mp = es("Mp", [P, 3, HEADS, G], BF16)
                Mrest = es("Mrest", [P, HEADS, G])
                sarg = es("sarg", [P, HEADS])
                sc = es("sc", [P, HEADS])
                arg = es("arg", [P, G, HEADS])
                pA = [pb(f"pA{i}", [P, 512], F32, edge) for i in two]
                pB = pb("pB", [P, 512], F32, edge)
                pT = [pb(f"pT{i}", [P, 1024], BF16, edge) for i in two]
                pC = [pb(f"pC{i}", [P, 512], F32, edge) for i in two]
                es_ = lambda name: sem(name, edge)
                sd_landed = [es_(f"sd_landed{i}") for i in two]
                attr_landed = es_("attr_landed")
                g_landed = [es_(f"g_landed{i}") for i in two]
                S = Counts(es_,
                           sp="fetch_begun",
                           pool="gather_begun",
                           dve="init sd_taken src_ready dloc_ready dst_ready oh_ready dt_copied steps_done end_ready "
                               "pen_ready logit_sum alpha_ready scanned runend_ready end0_ready endr_ready end1_ready "
                               "ends_ready absent_ready mt_ready mr_ready f_done r_done max_ready mp0_ready mpr_ready "
                               "mp1_ready mp_ready diff_ready carry_ready sarg0_ready sarg_ready arg_ready weighted "
                               "acc_done rescaled",
                           act="turned_copied pens_ready oh_wide sc_ready ea_ready",
                           pe="sd_turned turned logits_done dt_turned alpha_turned ends_turned segmax_done "
                              "shift_done agg_done")
                FILLS = 2 + 2

                with nc.Block() as block:
                    @block.sync
                    def _(sp):
                        def fetch(q, first):
                            rows = [sp.value_load(edge_row[0:1, bass.ds(q.times(G, t), 1)],
                                                  min_val=0, max_val=E - P) for t in range(G)]
                            if not first:
                                S.wait(sp, "turned", q.times(FILLS, 2 - FILLS))
                                sp.sem_inc(S["fetch_begun"], 1)
                            for t in range(G):
                                e0 = rows[t]
                                sp.dma_start(SDi[q.slot][2 * t:2 * t + 2, :], edges[:, bass.ds(e0, P)]
                                             ).then_inc(sd_landed[q.slot], DMA)
                                sp.dma_start(AT[:, t, :], edge_attr[bass.ds(e0, P), :]
                                             ).then_inc(attr_landed, DMA)

                        S.start(sp, "sp")
                        fetch(Step(None, 0), True)
                        two_step_loop(sp, GROUPS, lambda q: fetch(q.next(), False))

                    @block.gpsimd
                    def _(pool):
                        def gather(q):
                            S.wait(pool, "src_ready", q.times(1, 1))
                            pool.sem_inc(S["gather_begun"], 1)
                            for t in range(G):
                                nc.gpsimd.indirect_dma_start(
                                    out=gath[q.slot][:, t, :], out_offset=None, in_=table[:, :],
                                    in_offset=bass.IndirectOffsetOnAxis(ap=srcI[q.slot][:, t:t + 1], axis=0),
                                ).then_inc(g_landed[q.slot], DMA)

                        S.start(pool, "pool")
                        two_step_loop(pool, GROUPS, gather)

                    def flat(a):
                        return a.rearrange("p a b -> p (a b)")

                    @block.vector
                    def _(dve):
                        v = nc.vector

                        def when(name, value):
                            S.wait(dve, name, value)

                        S.start(dve, "dve")
                        v.memset(SDf[:, :], 0.0)
                        for i in two:
                            v.memset(penF[i][:, :, 0], -BIG)
                            v.memset(penR[i][:, :, G - 1], -BIG)
                        v.memset(seg_pen[0][:, 0:1], -BIG)
                        v.memset(seg_pen[1][:, 0:1], -BIG)
                        v.memset(seg_end[0][:, P - 1:P], 1.0)
                        v.memset(seg_end[1][:, P - 1:P], 1.0)
                        v.memset(mF[:, :, 0], -BIG).then_inc(S["init"], 1)
                        when("init", 1)

                        def ids_to_float(q):
                            dve.wait_ge(sd_landed[q.slot], q.uses(G * DMA))
                            when("sd_turned", q.times(1))
                            v.tensor_copy(SDf[0:2 * G, :], SDi[q.slot][:, :]).then_inc(S["sd_taken"], 1)

                        def ids_by_edge(q):
                            when("sd_turned", q.times(1, 1))
                            ids = pA[q.slot][:, 0:2 * G].rearrange("p (t two) -> p t two", two=2)
                            v.tensor_copy(srcI[q.slot][:, :], ids[:, :, 0]).then_inc(S["src_ready"], 1)
                            v.tensor_tensor(dloc[:, :], ids[:, :, 1], geo[:, bass.ds(q.times(G), G)], ALU.subtract
                                            ).then_inc(S["dloc_ready"], 1)
                            v.tensor_copy(dst8[:, :, :], ids[:, :, 1].unsqueeze(2).broadcast_to([P, G, HEADS])
                                          ).then_inc(S["dst_ready"], 1)

                        def one_hot(q):
                            when("dloc_ready", q.times(1, 1))
                            v.tensor_tensor(OHb[q.slot][:, :, :],
                                            iota_row[:, :].unsqueeze(1).broadcast_to([P, G, P]),
                                            dloc[:, :].unsqueeze(2).broadcast_to([P, G, P]), ALU.is_equal
                                            ).then_inc(S["oh_ready"], 1)

                        def segments(q):
                            when("dt_turned", q.times(1, 1))
                            v.tensor_copy(dT[:, :], pA[q.slot][:, P + GH:P + GH + P]
                                          ).then_inc(S["dt_copied"], 1)
                            when("dt_copied", q.times(1, 1))
                            v.tensor_tensor(step_[:, 1:P], dT[:, 1:P], dT[:, 0:P - 1], ALU.subtract
                                            ).then_inc(S["steps_done"], 1)
                            when("steps_done", q.times(1, 1))
                            v.tensor_scalar(seg_end[q.slot][:, 0:P - 1], step_[:, 1:P], 0.0, None, ALU.not_equal
                                            ).then_inc(S["end_ready"], 1)
                            v.tensor_scalar(seg_pen[q.slot][:, 1:P], step_[:, 1:P], 0.0, -BIG, ALU.not_equal,
                                            ALU.mult).then_inc(S["pen_ready"], 1)

                        def step(q):
                            nx = q.next()
                            done = q.times(1, 1)
                            dve.wait_ge(g_landed[q.slot], q.uses(G * DMA))
                            when("logits_done", done)
                            g4 = gath[q.slot][:, :, :].rearrange("p t (h c) -> p t h c", c=CW)
                            v.tensor_tensor(al0[:, :, :], pA[q.slot][:, P:P + GH].rearrange(
                                "p (t h) -> p t h", h=HEADS), g4[:, :, :, C], ALU.add).then_inc(S["logit_sum"], 1)
                            ids_to_float(nx)
                            when("logit_sum", done)
                            v.scalar_tensor_tensor(al[:, :, :], al0[:, :, :], SLOPE, al0[:, :, :], ALU.mult, ALU.max
                                                   ).then_inc(S["alpha_ready"], 1)
                            ids_by_edge(nx)
                            when("alpha_turned", done)
                            when("pen_ready", done)
                            v.tensor_tensor_scan(run[:, :], seg_pen[q.slot][:, :], pB[:, 0:P], -BIG, ALU.add, ALU.max
                                                 ).then_inc(S["scanned"], 1)
                            when("scanned", done)
                            v.tensor_tensor(runend[:, :], run[:, :], seg_end[q.slot][:, :], ALU.mult
                                            ).then_inc(S["runend_ready"], 1)
                            one_hot(nx)
                            when("ends_turned", done)
                            part = [endp[:, i, :, :].rearrange("p t h -> p (t h)") for i in range(4)]
                            v.tensor_copy(part[0], pB[:, P:2 * P]).then_inc(S["end0_ready"], 1)
                            v.tensor_copy(part[3], pB[:, 2 * P:3 * P])
                            when("end0_ready", done)
                            v.tensor_tensor(rest[:, :], pB[:, P:2 * P], part[0], ALU.subtract
                                            ).then_inc(S["endr_ready"], 1)
                            when("endr_ready", done)
                            v.tensor_copy(part[1], rest[:, :]).then_inc(S["end1_ready"], 1)
                            when("end1_ready", done)
                            v.tensor_tensor(part[2], rest[:, :], part[1], ALU.subtract
                                            ).then_inc(S["ends_ready"], 1)
                            when("segmax_done", done)
                            v.tensor_scalar(absent[:, :, :], pB[:, GH:2 * GH].rearrange("p (t h) -> p t h", h=HEADS),
                                            BIG, -BIG, ALU.mult, ALU.add).then_inc(S["absent_ready"], 1)
                            when("absent_ready", done)
                            when("carry_ready", q.times(1))
                            v.tensor_tensor(mF[:, :, 1:G + 1], pB[:, 0:GH].rearrange("p (t h) -> p h t", h=HEADS),
                                            absent[:, :, :].rearrange("p t h -> p h t"), ALU.add
                                            ).then_inc(S["mt_ready"], 1)
                            when("mt_ready", done)
                            when("pens_ready", done)
                            v.tensor_copy(mR[:, :, :], mF[:, :, 1:G + 1]).then_inc(S["mr_ready"], 1)
                            v.tensor_tensor_scan(flat(F[:, :, :]), flat(penF[q.slot][:, :, :]), flat(mF[:, :, :]),
                                                 -BIG, ALU.add, ALU.max).then_inc(S["f_done"], 1)
                            when("mr_ready", done)
                            v.tensor_tensor_scan(flat(R[:, :, :])[:, ::-1], flat(penR[q.slot][:, :, :])[:, ::-1],
                                                 flat(mR[:, :, :])[:, ::-1], -BIG, ALU.add, ALU.max
                                                 ).then_inc(S["r_done"], 1)
                            when("r_done", done)
                            when("f_done", done)
                            v.tensor_tensor(M[:, :, :], F[:, :, 1:G + 1], R[:, :, :], ALU.max
                                            ).then_inc(S["max_ready"], 1)
                            when("max_ready", done)
                            v.tensor_copy(Mp[:, 0, :, :], M[:, :, :]).then_inc(S["mp0_ready"], 1)
                            v.tensor_tensor(sarg[:, :], mF[:, :, 0], M[:, :, 0], ALU.subtract
                                            ).then_inc(S["sarg0_ready"], 1)
                            when("mp0_ready", done)
                            v.tensor_tensor(Mrest[:, :, :], M[:, :, :], Mp[:, 0, :, :], ALU.subtract
                                            ).then_inc(S["mpr_ready"], 1)
                            when("sarg0_ready", done)
                            v.tensor_copy(mF[:, :, 0], M[:, :, G - 1]).then_inc(S["carry_ready"], 1)
                            when("mpr_ready", done)
                            v.tensor_copy(Mp[:, 1, :, :], Mrest[:, :, :]).then_inc(S["mp1_ready"], 1)
                            when("mp1_ready", done)
                            v.tensor_tensor(Mp[:, 2, :, :], Mrest[:, :, :], Mp[:, 1, :, :], ALU.subtract
                                            ).then_inc(S["mp_ready"], 1)
                            when("sc_ready", q.times(1))
                            v.tensor_scalar(sarg[:, :], sarg[:, :], penb[:, bass.ds(q.times(G), 1)], None, ALU.add
                                            ).then_inc(S["sarg_ready"], 1)
                            when("shift_done", done)
                            v.tensor_tensor(arg[:, :, :], al[:, :, :],
                                            pB[:, 3 * P:3 * P + GH].rearrange("p (t h) -> p t h", h=HEADS),
                                            ALU.subtract).then_inc(S["diff_ready"], 1)
                            when("diff_ready", done)
                            v.tensor_scalar_min(arg[:, :, :], arg[:, :, :], 0.0).then_inc(S["arg_ready"], 1)
                            off0 = dve.value_load(acc_off[0:1, bass.ds(q.times(G), 1)],
                                                  min_val=0, max_val=(NT - 1) * TW)
                            when("sc_ready", done)
                            when("acc_done", q.times(G))
                            head = acc[:, bass.ds(off0, TW)].rearrange("p (h c) -> p h c", c=CW)
                            v.tensor_tensor(head, head, sc[:, :].unsqueeze(2).broadcast_to([P, HEADS, CW]), ALU.mult
                                            ).then_inc(S["rescaled"], 1)
                            when("ea_ready", done)

                            def weigh(t):
                                v.tensor_tensor(g4[:, t, :, 0:C], g4[:, t, :, 0:C],
                                                g4[:, t, :, C].unsqueeze(2).broadcast_to([P, HEADS, C]), ALU.mult
                                                ).then_inc(S["weighted"], 1)

                            weigh(0)
                            weigh(1)
                            for t in range(G):
                                if t + 2 < G:
                                    weigh(t + 2)
                                off = dve.value_load(acc_off[0:1, bass.ds(q.times(G, t), 1)],
                                                     min_val=0, max_val=(NT - 1) * TW)
                                when("agg_done", q.times(G, t + 1))
                                when("acc_done", q.times(G, t))
                                if t == 0:
                                    when("rescaled", done)
                                a = acc[:, bass.ds(off, TW)]
                                v.tensor_tensor(a, a, pC[t % 2][:, 0:TW], ALU.add).then_inc(S["acc_done"], 1)
                            segments(nx)

                        q0 = Step(None, 0)
                        ids_to_float(q0)
                        ids_by_edge(q0)
                        one_hot(q0)
                        segments(q0)
                        two_step_loop(dve, GROUPS, step)

                    @block.scalar
                    def _(act):
                        def prepare(q, first):
                            S.wait(act, "init", 1)
                            p16 = penb[:, bass.ds(q.times(G), G)].unsqueeze(1).broadcast_to([P, HEADS, G])
                            p15 = penb[:, bass.ds(q.times(G, 1), G - 1)].unsqueeze(1).broadcast_to([P, HEADS, G - 1])
                            if not first:
                                S.wait(act, "max_ready", q.times(1, -1))
                            nc.scalar.copy(penF[q.slot][:, :, 1:G + 1], p16)
                            nc.scalar.copy(penR[q.slot][:, :, 0:G - 1], p15).then_inc(S["pens_ready"], 1)
                            if not first:
                                S.wait(act, "shift_done", q.times(1, -1))
                                S.wait(act, "logits_done", q.times(1))
                            for f in range(FILLS):
                                S.wait(act, "turned", q.times(FILLS, f + 1))
                                if f < 2:
                                    nc.scalar.copy(ATT[:, 4 * f:4 * f + 4, :],
                                                   pT[f % 2][:, :].bitcast(F32).rearrange("p (a b) -> p a b", b=P)
                                                   ).then_inc(S["turned_copied"], 1)
                                else:
                                    nc.scalar.copy(OHT[q.slot][:, 8 * (f - 2):8 * (f - 2) + 8, :],
                                                   pT[f % 2][:, :].rearrange("p (a b) -> p a b", b=P)
                                                   ).then_inc(S["turned_copied"], 1)

                        def widen(q):
                            S.wait(act, "oh_ready", q.times(1, 1))
                            S.wait(act, "agg_done", q.times(G))
                            for k in range(4):
                                nc.scalar.copy(OH[:, 4 * k:4 * k + 4, :], OHb[q.slot][:, 4 * k:4 * k + 4, :]
                                               ).then_inc(S["oh_wide"], 1)

                        def step(q):
                            widen(q)
                            prepare(q.next(), False)
                            done = q.times(1, 1)
                            S.wait(act, "sarg_ready", done)
                            S.wait(act, "rescaled", q.times(1))
                            nc.scalar.activation(sc[:, :], sarg[:, :], ACT.Exp).then_inc(S["sc_ready"], 1)
                            S.wait(act, "arg_ready", done)
                            g4 = gath[q.slot][:, :, :].rearrange("p t (h c) -> p t h c", c=CW)
                            nc.scalar.activation(g4[:, :, :, C], arg[:, :, :], ACT.Exp).then_inc(S["ea_ready"], 1)

                        S.start(act, "act")
                        prepare(Step(None, 0), True)
                        two_step_loop(act, GROUPS, step)

                    @block.tensor
                    def _(pe):
                        def when(name, value):
                            S.wait(pe, name, value)

                        def turn_ids(q):
                            when("sd_taken", q.times(1, 1))
                            nc.tensor.transpose(pA[q.slot][:, 0:P], SDf[:, :], ident[:, :]
                                                ).then_inc(S["sd_turned"], 1)

                        def fill(q, f, first):
                            if not (first and f < 2):
                                when("turned_copied", q.times(FILLS, f - 1))
                            if f < 2:
                                for i in range(4):
                                    t = 2 * (4 * f + i)
                                    last = nc.tensor.transpose(pT[f][:, :].bitcast(F32)[:, i * P:(i + 1) * P],
                                                               AT[:, t:t + 2, :].rearrange("p t a -> p (t a)"),
                                                               ident[:, :])
                            else:
                                for i in range(8):
                                    last = nc.tensor.transpose(pT[f % 2][:, i * P:(i + 1) * P],
                                                               OHb[q.slot][:, 8 * (f - 2) + i, :], identb[:, :])
                            last.then_inc(S["turned"], 1)

                        def turn_attr(q, first):
                            pe.wait_ge(attr_landed, q.times(G * DMA, G * DMA))
                            for f in range(2):
                                fill(q, f, first)

                        def turn_one_hot(q, first):
                            when("oh_ready", q.times(1, 1))
                            for f in range(2, FILLS):
                                fill(q, f, first)

                        def logits(q):
                            offs = [pe.value_load(ad_off[0:1, bass.ds(q.times(G, t), 1)],
                                                  min_val=0, max_val=(NT - 1) * HEADS) for t in range(G)]
                            when("dst_ready", q.times(1, 1))
                            when("turned_copied", q.times(FILLS, FILLS))
                            for t in range(0, G, 2):
                                nc.tensor.matmul(pA[q.slot][:, P + t * HEADS:P + (t + 2) * HEADS], ATT[:, t // 2, :],
                                                 We8[:, :, :].rearrange("p a h -> p (a h)"),
                                                 start=(t == 0), stop=False)
                            for t in range(G):
                                for i in range(3):
                                    last = nc.tensor.matmul(pA[q.slot][:, P + t * HEADS:P + (t + 1) * HEADS],
                                                            OHT[q.slot][:, t, :],
                                                            AD3[:, i, bass.ds(offs[t], HEADS)],
                                                            start=False, stop=(t == G - 1 and i == 2))
                            last.then_inc(S["logits_done"], 1)
                            nc.tensor.transpose(pA[q.slot][:, P + GH:P + GH + P],
                                                dst8[:, :, :].rearrange("p t h -> p (t h)"), ident[:, :]
                                                ).then_inc(S["dt_turned"], 1)

                        def step(q):
                            nx = q.next()
                            done = q.times(1, 1)
                            turn_ids(nx)
                            when("alpha_ready", done)
                            nc.tensor.transpose(pB[:, 0:P], al[:, :, :].rearrange("p t h -> p (t h)"), ident[:, :]
                                                ).then_inc(S["alpha_turned"], 1)
                            turn_attr(nx, False)
                            when("runend_ready", done)
                            nc.tensor.transpose(pB[:, P:2 * P], runend[:, :], ident[:, :])
                            nc.tensor.transpose(pB[:, 2 * P:3 * P], seg_end[q.slot][:, :], ident[:, :]
                                                ).then_inc(S["ends_turned"], 1)
                            when("ends_ready", done)
                            m_out = pB[:, 0:2 * GH].rearrange("p (a t h) -> p a t h", a=2, h=HEADS)
                            for t in range(G):
                                nc.tensor.matmul(m_out[:, :, t, :], OHb[q.slot][:, t, :], endp[:, 0:4:3, t, :],
                                                 start=(t == 0), stop=False)
                                nc.tensor.matmul(m_out[:, 0, t, :], OHb[q.slot][:, t, :], endp[:, 1, t, :],
                                                 start=False, stop=False)
                                last = nc.tensor.matmul(m_out[:, 0, t, :], OHb[q.slot][:, t, :], endp[:, 2, t, :],
                                                        start=False, stop=(t == G - 1))
                            last.then_inc(S["segmax_done"], 1)
                            turn_one_hot(nx, False)
                            when("mp_ready", done)
                            for t in range(G):
                                for i in range(3):
                                    last = nc.tensor.matmul(pB[:, 3 * P + t * HEADS:3 * P + (t + 1) * HEADS],
                                                            OHT[q.slot][:, t, :], Mp[:, i, :, t],
                                                            start=(t == 0 and i == 0),
                                                            stop=(t == G - 1 and i == 2))
                            last.then_inc(S["shift_done"], 1)
                            logits(nx)
                            for t in range(G):
                                when("weighted", q.times(G, t + 1))
                                if t % 4 == 0:
                                    when("oh_wide", q.times(4, t // 4 + 1))
                                if t >= 2:
                                    when("acc_done", q.times(G, t - 1))
                                nc.tensor.matmul(pC[t % 2][:, 0:TW], OH[:, t, :], gath[q.slot][:, t, :],
                                                 start=True, stop=True).then_inc(S["agg_done"], 1)

                        S.start(pe, "pe")
                        q0 = Step(None, 0)
                        turn_ids(q0)
                        turn_attr(q0, True)
                        turn_one_hot(q0, True)
                        logits(q0)
                        two_step_loop(pe, GROUPS, step)

        late = ExitStack()
        with late:
            ls = lambda name, shape, dt=F32: sb(name, shape, dt, late)
            b1_b = ls("b1_b", [P, NX * HID])
            b2_b = ls("b2_b", [P, NX * D])
            pos_i = ls("pos_i", [P, 2, NT], I32)
            w_top = ls("w_top", [P, 2, NT])
            w_off = ls("w_off", [1, XS + 2], I32)
            b1_off = ls("b1_off", [1, XS + 2], I32)
            b2_off = ls("b2_off", [1, XS + 2], I32)
            need_w = ls("need_w", [1, 2, XS + 2], I32)
            t_end = ls("t_end", [1, NX], I32)
            biases_in = sem("biases_in", late)

            route = ExitStack()
            with route:
                rs = lambda name, shape, dt=F32: sb(name, shape, dt, route)
                bias_b = rs("bias_b", [P, D])
                gamma_b = rs("gamma_b", [P, D])
                beta_b = rs("beta_b", [P, D])
                affine_in = sem("affine_in", route)
                den = rs("den", [P, NT, HEADS])
                Y = rs("Y", [P, NT, D])
                ZT = rs("ZT", [P, 2, KD, P])
                Wg_s = rs("Wg_s", [P, KD, NX])
                bg_b = rs("bg_b", [P, NX])
                logit = rs("logit", [P, NT, NX])
                top8 = rs("top8", [P, NT, 8])
                idx8 = rs("idx8", [P, NT, 8], U32)
                idxf = rs("idxf", [P, NT, 2])
                live = rs("live", [P, NT])
                sel = rs("sel", [P, 2, NT, NX])
                both = rs("both", [P, NT, NX])
                earlier = rs("earlier", [P, NT + 1, NX])
                place = rs("place", [P, NT, NX])
                pick = rs("pick", [P, 2, NT, NX])
                posf = rs("posf", [P, 2, NT])
                tot = rs("tot", [P, 6, NX])
                toti = rs("toti", [P, 2, NX], I32)
                wtmp = rs("wtmp", [P, 4, NT])
                srow = rs("srow", [1, 4, XS + 2])
                iota_s = rs("iota_s", [1, XS + 2])
                pZ = [pb(f"pZ{i}", [P, 512], F32, route) for i in range(2)]
                pL = [pb(f"pL{i}", [P, 512], F32, route) for i in range(2)]
                pR = pb("pR", [P, 512], F32, route)
                pQ = pb("pQ", [P, 512], F32, route)
                rsem = lambda name: sem(name, route)
                gate_in = rsem("gate_in")
                order = rsem("order")
                s_iota = rsem("s_iota")
                var1 = rsem("var1")
                std1 = rsem("std1")
                var2 = rsem("var2")
                std2 = rsem("std2")
                z_done = rsem("z_done")
                zt_turned = rsem("zt_turned")
                zt_copied = rsem("zt_copied")
                gate_done = rsem("gate_done")
                gate_copied = rsem("gate_copied")
                gap_done = rsem("gap_done")
                ratio_done = rsem("ratio_done")
                sel_done = rsem("sel_done")
                ranked = rsem("ranked")
                pos_done = rsem("pos_done")
                sent = rsem("sent")

                with nc.Block() as block:
                    @block.sync
                    def _(sp):
                        for b, a in ((bias_b, g_bias), (gamma_b, g_gamma), (beta_b, g_beta)):
                            sp.dma_start(b[:, :], a.partition_broadcast(P)).then_inc(affine_in, DMA)
                        sp.dma_start(Wg_s[:, :, :], Wg.rearrange("(k p) e -> p k e", p=P)).then_inc(gate_in, DMA)
                        sp.dma_start(bg_b[:, :], bg.partition_broadcast(P)).then_inc(gate_in, DMA)
                        sp.dma_start(b1_b[:, :], b1.rearrange("e n -> (e n)").partition_broadcast(P)
                                     ).then_inc(biases_in, DMA)
                        sp.dma_start(b2_b[:, :], b2.rearrange("e n -> (e n)").partition_broadcast(P)
                                     ).then_inc(biases_in, DMA)

                    @block.gpsimd
                    def _(pool):
                        nc.gpsimd.memset(live[:, :], 1.0)
                        nc.gpsimd.iota(iota_s[:, :], pattern=[[1, XS + 2]], base=0, channel_multiplier=0,
                                       allow_small_or_imprecise_dtypes=True).then_inc(s_iota, 1)
                        pool.wait_ge(s_iota, 1)
                        nc.gpsimd.affine_select(out=live[:, NT - 1:NT], in_=live[:, NT - 1:NT], compare_op=ALU.is_gt,
                                                fill=0.0, base=LAST, pattern=[[0, 1]], channel_multiplier=-1
                                                ).then_inc(s_iota, 1)
                        pool.wait_ge(pos_done, 1)
                        for t in range(NT):
                            for k in range(2):
                                nc.gpsimd.indirect_dma_start(
                                    out=slots_in[:, :],
                                    out_offset=bass.IndirectOffsetOnAxis(ap=pos_i[:, k, t:t + 1], axis=0),
                                    in_=XN[:, t, :], in_offset=None,
                                    bounds_check=XS * P - 1, oob_is_err=False).then_inc(sent, DMA)
                        pool.wait_ge(sent, 2 * NT * DMA)

                    @block.vector
                    def _(dve):
                        v = nc.vector
                        n = [0]

                        def run_(ins):
                            n[0] += 1
                            ins.then_inc(order, 1)

                        def sync():
                            dve.wait_ge(order, n[0])

                        def norm_stats(done):
                            for t in range(NT):
                                run_(v.bn_stats(stats[:, t, :], Y[:, t, :]))
                            sync()
                            for t in range(NT):
                                last = v.bn_aggr(mv[:, t, :], stats[:, t, :])
                            last.then_inc(done, 1)

                        run_(v.tensor_scalar_add(den[:, :, :], acc_v[:, :, :, C], 1e-16))
                        sync()
                        run_(v.reciprocal(den[:, :, :], den[:, :, :]))
                        sync()
                        for t in range(NT):
                            run_(v.tensor_tensor(Y[:, t, :].rearrange("p (h c) -> p h c", c=C), acc_v[:, t, :, 0:C],
                                                 den[:, t, :].unsqueeze(2).broadcast_to([P, HEADS, C]), ALU.mult))
                        sync()
                        for t in range(NT):
                            run_(v.tensor_tensor(Y[:, t, :], Y[:, t, :], XN[:, t, :], ALU.add))
                        sync()
                        dve.wait_ge(affine_in, 3 * DMA)
                        for t in range(NT):
                            run_(v.tensor_tensor(Y[:, t, :], Y[:, t, :], bias_b[:, :], ALU.add))
                        sync()
                        norm_stats(var1)
                        dve.wait_ge(std1, 1)
                        run_(v.reciprocal(rstd[:, :], rstd[:, :]))
                        sync()
                        for t in range(NT):
                            run_(v.tensor_scalar(Y[:, t, :], Y[:, t, :], mv[:, t, 0:1], rstd[:, t:t + 1],
                                                 ALU.subtract, ALU.mult))
                        sync()
                        for t in range(NT):
                            run_(v.tensor_tensor(Y[:, t, :], Y[:, t, :], gamma_b[:, :], ALU.mult))
                        sync()
                        for t in range(NT):
                            run_(v.tensor_tensor(X[:, t, :], X[:, t, :], beta_b[:, :], ALU.add))
                        sync()
                        for t in range(NT):
                            run_(v.tensor_tensor(Y[:, t, :], Y[:, t, :], X[:, t, :], ALU.add))
                        sync()
                        norm_stats(var2)
                        dve.wait_ge(std2, 1)
                        run_(v.reciprocal(rstd[:, :], rstd[:, :]))
                        sync()
                        for t in range(NT):
                            v.tensor_scalar(XN[:, t, :], Y[:, t, :], mv[:, t, 0:1], rstd[:, t:t + 1],
                                            ALU.subtract, ALU.mult).then_inc(z_done, 1)
                        for t in range(NT):
                            run_(v.tensor_copy(X[:, t, :], Y[:, t, :]))
                        dve.wait_ge(gate_in, 2 * DMA)
                        for t in range(NT):
                            dve.wait_ge(gate_done, t + 1)
                            v.tensor_tensor(logit[:, t, :], pL[t % 2][:, 0:NX], bg_b[:, :], ALU.add
                                            ).then_inc(gate_copied, 1)
                        dve.wait_ge(gate_copied, NT)
                        for t in range(NT):
                            run_(v.max(top8[:, t, :], logit[:, t, :]))
                        sync()
                        for t in range(NT):
                            run_(v.max_index(idx8[:, t, :], top8[:, t, :], logit[:, t, :]))
                        sync()
                        v.tensor_tensor(wtmp[:, 0, :], top8[:, :, 1], top8[:, :, 0], ALU.subtract).then_inc(gap_done, 1)
                        run_(v.tensor_copy(idxf[:, :, :], idx8[:, :, 0:2]))
                        sync()
                        for k in range(2):
                            run_(v.tensor_tensor(sel[:, k, :, :],
                                                 iota_row[:, 0:NX].unsqueeze(1).broadcast_to([P, NT, NX]),
                                                 idxf[:, :, k].unsqueeze(2).broadcast_to([P, NT, NX]), ALU.is_equal))
                        sync()
                        dve.wait_ge(s_iota, 2)
                        for k in range(2):
                            run_(v.tensor_tensor(sel[:, k, :, :], sel[:, k, :, :],
                                                 live[:, :].unsqueeze(2).broadcast_to([P, NT, NX]), ALU.mult))
                        sync()
                        run_(v.tensor_tensor(both[:, :, :], sel[:, 0, :, :], sel[:, 1, :, :], ALU.add))
                        run_(v.memset(earlier[:, 0, :], 0.0))
                        sync()
                        for t in range(NT):
                            run_(v.tensor_tensor(earlier[:, t + 1, :], earlier[:, t, :], both[:, t, :], ALU.add))
                            sync()
                        dve.sem_inc(sel_done, 1)
                        dve.wait_ge(ratio_done, 1)
                        run_(v.tensor_scalar_add(wtmp[:, 2, :], wtmp[:, 1, :], 1.0))
                        sync()
                        run_(v.reciprocal(w_top[:, 0, :], wtmp[:, 2, :]))
                        sync()
                        run_(v.tensor_tensor(w_top[:, 1, :], w_top[:, 0, :], wtmp[:, 1, :], ALU.mult))
                        dve.wait_ge(ranked, 1)
                        run_(v.tensor_scalar_add(toti[:, 0, :], pQ[:, 0:NX], float(P - 1)))
                        sync()
                        run_(v.tensor_single_scalar(toti[:, 1, :], toti[:, 0, :], 7, ALU.arith_shift_right))
                        sync()
                        run_(v.tensor_copy(tot[:, 0, :], toti[:, 1, :]))
                        sync()
                        run_(v.tensor_tensor_scan(tot[:, 1, :], ones[:, 0:NX], tot[:, 0, :], 0.0, ALU.mult, ALU.add))
                        sync()
                        run_(v.tensor_tensor(tot[:, 2, :], tot[:, 1, :], tot[:, 0, :], ALU.subtract))
                        sync()
                        run_(v.tensor_scalar_mul(tot[:, 3, :], tot[:, 2, :], float(P)))
                        sync()
                        run_(v.tensor_tensor(place[:, :, :], pR[:, 0:NT * NX].rearrange("p (t e) -> p t e", e=NX),
                                             tot[:, 3, :].unsqueeze(1).broadcast_to([P, NT, NX]), ALU.add))
                        sync()
                        for k in range(2):
                            run_(v.tensor_tensor(pick[:, k, :, :], sel[:, k, :, :], place[:, :, :], ALU.mult))
                        sync()
                        for k in range(2):
                            run_(v.tensor_reduce(posf[:, k, :], pick[:, k, :, :], axis=AX.X, op=ALU.add))
                        run_(v.tensor_scalar(wtmp[:, 3, :], live[:, :], -float(XS * P * 4), float(XS * P * 4),
                                             ALU.mult, ALU.add))
                        sync()
                        for k in range(2):
                            run_(v.tensor_tensor(pos_i[:, k, :], posf[:, k, :], wtmp[:, 3, :], ALU.add))
                        sync()
                        dve.sem_inc(pos_done, 1)
                        run_(v.memset(srow[:, 0, :], 0.0))
                        sync()
                        for e in range(NX - 1):
                            run_(v.scalar_tensor_tensor(srow[:, 0, :], iota_s[:, :], tot[0:1, 1, e:e + 1],
                                                        srow[:, 0, :], ALU.is_ge, ALU.add))
                            sync()
                        run_(v.tensor_copy(need_w[:, 1, :], srow[:, 0, :]))
                        sync()
                        run_(v.tensor_single_scalar(need_w[:, 0, :], need_w[:, 1, :], 1, ALU.arith_shift_right))
                        sync()
                        run_(v.tensor_copy(srow[:, 1, :], need_w[:, 0, :]))
                        sync()
                        run_(v.scalar_tensor_tensor(srow[:, 2, :], srow[:, 1, :], -2.0, srow[:, 0, :],
                                                    ALU.mult, ALU.add))
                        sync()
                        run_(v.tensor_tensor(srow[:, 3, :], srow[:, 1, :], srow[:, 2, :], ALU.add))
                        sync()
                        run_(v.tensor_scalar(need_w[:, 0, :], srow[:, 1, :], 1.0, 2.0 * DMA, ALU.add, ALU.mult))
                        run_(v.tensor_scalar(need_w[:, 1, :], srow[:, 3, :], 1.0, 2.0 * DMA, ALU.max, ALU.mult))
                        run_(v.tensor_scalar_mul(w_off[:, :], srow[:, 2, :], float(KD * HID + KH * D)))
                        run_(v.tensor_scalar_mul(b1_off[:, :], srow[:, 0, :], float(HID)))
                        run_(v.tensor_scalar_mul(b2_off[:, :], srow[:, 0, :], float(D)))
                        run_(v.tensor_copy(t_end[:, :], tot[0:1, 1, :]))

                    @block.scalar
                    def _(act):
                        act.wait_ge(var1, 1)
                        nc.scalar.activation(rstd[:, :], mv[:, :, 1], ACT.Sqrt, bias=eps[:, :]).then_inc(std1, 1)
                        act.wait_ge(var2, 1)
                        nc.scalar.activation(rstd[:, :], mv[:, :, 1], ACT.Sqrt, bias=eps[:, :]).then_inc(std2, 1)
                        for t in range(NT):
                            act.wait_ge(zt_turned, t + 1)
                            if t >= 2:
                                act.wait_ge(gate_done, t - 1)
                            nc.scalar.copy(ZT[:, t % 2, :, :], pZ[t % 2][:, 0:KD * P].rearrange("p (k n) -> p k n", k=KD)
                                           ).then_inc(zt_copied, 1)
                        act.wait_ge(gap_done, 1)
                        nc.scalar.activation(wtmp[:, 1, :], wtmp[:, 0, :], ACT.Exp).then_inc(ratio_done, 1)

                    @block.tensor
                    def _(pe):
                        pe.wait_ge(gate_in, 2 * DMA)
                        for t in range(NT):
                            pe.wait_ge(z_done, t + 1)
                            if t >= 2:
                                pe.wait_ge(zt_copied, t - 1)
                            for k in range(KD):
                                last = nc.tensor.transpose(pZ[t % 2][:, k * P:(k + 1) * P],
                                                           XN[:, t, k * P:(k + 1) * P], ident[:, :])
                            last.then_inc(zt_turned, 1)
                            pe.wait_ge(zt_copied, t + 1)
                            if t >= 2:
                                pe.wait_ge(gate_copied, t - 1)
                            for k in range(KD):
                                last = nc.tensor.matmul(pL[t % 2][:, 0:NX], ZT[:, t % 2, k, :], Wg_s[:, k, :],
                                                        start=(k == 0), stop=(k == KD - 1))
                            last.then_inc(gate_done, 1)
                        pe.wait_ge(sel_done, 1)
                        nc.tensor.matmul(pR[:, 0:NT * NX], before[:, :], both[:, :, :].rearrange("p t e -> p (t e)"),
                                         start=True, stop=False)
                        nc.tensor.matmul(pR[:, 0:NT * NX], ones[:, :],
                                         earlier[:, 0:NT, :].rearrange("p t e -> p (t e)"), start=False, stop=True)
                        nc.tensor.matmul(pQ[:, 0:NX], ones[:, :], earlier[:, NT, :], start=True, stop=True
                                         ).then_inc(ranked, 1)

            ffn = ExitStack()
            with ffn:
                fs = lambda name, shape, dt=F32: sb(name, shape, dt, ffn)
                two = range(2)
                Z = [fs(f"Z{i}", [P, D]) for i in two]
                ZTs = [fs(f"ZTs{i}", [P, KD, P]) for i in two]
                Hb = [fs(f"Hb{i}", [P, HID]) for i in two]
                Hg = [fs(f"Hg{i}", [P, HID]) for i in two]
                HT = [fs(f"HT{i}", [P, KH, P]) for i in two]
                Yo = [fs(f"Yo{i}", [P, D]) for i in two]
                pH = [[pb(f"pH{i}{k}", [P, 512], F32, ffn) for k in two] for i in two]
                pTz = pb("pTz", [P, 512], F32, ffn)
                pTh = [pb(f"pTh{k}", [P, 512], F32, ffn) for k in two]
                pY2 = pb("pY2", [P, 512], F32, ffn)
                fsem = lambda name: sem(name, ffn)
                z_landed = [fsem(f"z_landed{i}") for i in two]
                y_out = [fsem(f"y_out{i}") for i in two]
                T = Counts(fsem, pool="released", dve="z_copied biased y_ready", act="gelu_done h_copied",
                           pe="z_turned up_done h_turned down_done")
                WSTEP = KD * HID + KH * D

                with nc.Block() as block:
                    @block.sync
                    def _(sp):
                        def fetch(i, first):
                            row = sp.snap(i.times(P))
                            if not first:
                                T.wait(sp, "z_turned", i.times(1, -1))
                            sp.dma_start(Z[i.slot][:, :], slots_in[bass.ds(row, P), :]
                                         ).then_inc(z_landed[i.slot], DMA)

                        def store(i):
                            row = sp.snap(i.times(P))
                            T.wait(sp, "y_ready", i.times(1, 1))
                            sp.dma_start(slots_out[bass.ds(row, P), :], Yo[i.slot][:, :]
                                         ).then_inc(y_out[i.slot], DMA)

                        for i in two:
                            sp.sem_inc(y_out[i], DMA)
                        fetch(Step(None, 0), True)
                        fetch(Step(None, 1), True)

                        def step(i):
                            fetch(i.next().next(), False)
                            store(i)

                        two_step_loop(sp, XS, step)
                        for i in two:
                            sp.wait_ge(y_out[i], (XS // 2 + 1) * DMA)

                    @block.gpsimd
                    def _(pool):
                        T.start(pool, "pool")
                        for e in range(2, NX):
                            done = pool.value_load(t_end[0:1, e - 2:e - 1], min_val=0, max_val=XS)
                            T.wait(pool, "down_done", done)
                            pool.sem_inc(T["released"], 1)
                            pool.wait_ge(expert_w[e % 2], (e // 2) * 2 * DMA)
                            load_expert(pool, e, e % 2)

                    @block.scalar
                    def _(act):
                        T.start(act, "act")

                        def step(i):
                            T.wait(act, "biased", i.times(1, 1))
                            T.wait(act, "h_turned", i.times(1))
                            nc.scalar.activation(Hg[i.slot][:, :], Hb[i.slot][:, :], ACT.Gelu
                                                 ).then_inc(T["gelu_done"], 1)
                            T.wait(act, "h_turned", i.times(1, 1))
                            for k in two:
                                last = nc.scalar.copy(HT[i.slot][:, 4 * k:4 * k + 4, :],
                                                      pTh[k][:, :].rearrange("p (a b) -> p a b", b=P))
                            last.then_inc(T["h_copied"], 1)

                        two_step_loop(act, XS, step)

                    @block.vector
                    def _(dve):
                        v = nc.vector
                        dve.wait_ge(biases_in, 2 * DMA)

                        T.start(dve, "dve")

                        def z_copy(i):
                            T.wait(dve, "z_turned", i.times(1, 1))
                            v.tensor_copy(ZTs[i.slot][:, :, :], pTz[:, 0:KD * P].rearrange("p (k n) -> p k n", k=KD)
                                          ).then_inc(T["z_copied"], 1)

                        def bias(i, first):
                            off = dve.value_load(b1_off[0:1, bass.ds(i.times(1), 1)],
                                                 min_val=0, max_val=(NX - 1) * HID)
                            T.wait(dve, "up_done", i.times(1, 1))
                            if not first:
                                T.wait(dve, "gelu_done", i.times(1, -1))
                            for k in two:
                                last = v.tensor_tensor(Hb[i.slot][:, k * 512:(k + 1) * 512], pH[i.slot][k][:, :],
                                                       b1_b[:, bass.ds(off + k * 512, 512)], ALU.add)
                            last.then_inc(T["biased"], 1)

                        def step(i):
                            off = dve.value_load(b2_off[0:1, bass.ds(i.times(1), 1)], min_val=0, max_val=(NX - 1) * D)
                            bias(i.next(), False)
                            z_copy(i.next().next())
                            T.wait(dve, "down_done", i.times(1, 1))
                            dve.wait_ge(y_out[i.slot], i.uses(DMA))
                            v.tensor_tensor(Yo[i.slot][:, :], pY2[:, 0:D], b2_b[:, bass.ds(off, D)], ALU.add
                                            ).then_inc(T["y_ready"], 1)

                        z_copy(Step(None, 0))
                        bias(Step(None, 0), True)
                        z_copy(Step(None, 1))
                        two_step_loop(dve, XS, step)

                    @block.tensor
                    def _(pe):
                        T.start(pe, "pe")
                        wf = wbuf[:, :, :].rearrange("p s n -> p (s n)")

                        def turn_z(i, first):
                            pe.wait_ge(z_landed[i.slot], i.uses(DMA))
                            if not first:
                                T.wait(pe, "z_copied", i.times(1))
                            for k in range(KD):
                                last = nc.tensor.transpose(pTz[:, k * P:(k + 1) * P], Z[i.slot][:, k * P:(k + 1) * P],
                                                           ident[:, :])
                            last.then_inc(T["z_turned"], 1)

                        def expert(i):
                            off = pe.value_load(w_off[0:1, bass.ds(i.times(1), 1)], min_val=0, max_val=WSTEP)
                            need = [pe.value_load(need_w[0:1, s, bass.ds(i.times(1), 1)], min_val=0, max_val=NX * DMA)
                                    for s in two]
                            for s in two:
                                pe.wait_ge(expert_w[s], need[s])
                            return off

                        def up(i, n, off):
                            for k in range(KD):
                                last = nc.tensor.matmul(pH[i.slot][n][:, :], ZTs[i.slot][:, k, :],
                                                        wf[:, bass.ds(off + (k * HID + n * 512), 512)],
                                                        start=(k == 0), stop=(k == KD - 1))
                            return last

                        def step(i):
                            nx = i.next()
                            down_off = pe.value_load(w_off[0:1, bass.ds(i.times(1), 1)], min_val=0, max_val=WSTEP)
                            off = expert(nx)
                            T.wait(pe, "z_copied", nx.times(1, 1))
                            T.wait(pe, "biased", nx.times(1, -1))
                            up(nx, 0, off)
                            T.wait(pe, "gelu_done", i.times(1, 1))
                            T.wait(pe, "h_copied", i.times(1))
                            for c in range(KH):
                                last = nc.tensor.transpose(pTh[c // 4][:, (c % 4) * P:(c % 4 + 1) * P],
                                                           Hg[i.slot][:, c * P:(c + 1) * P], ident[:, :])
                            last.then_inc(T["h_turned"], 1)
                            up(nx, 1, off).then_inc(T["up_done"], 1)
                            turn_z(nx.next(), False)
                            T.wait(pe, "h_copied", i.times(1, 1))
                            T.wait(pe, "y_ready", i.times(1))
                            for c in range(KH):
                                last = nc.tensor.matmul(pY2[:, 0:D], HT[i.slot][:, c, :],
                                                        wf[:, bass.ds(down_off + (KD * HID + c * D), D)],
                                                        start=(c == 0), stop=(c == KH - 1))
                            last.then_inc(T["down_done"], 1)

                        turn_z(Step(None, 0), True)
                        T.wait(pe, "z_copied", 1)
                        off0 = expert(Step(None, 0))
                        up(Step(None, 0), 0, off0)
                        up(Step(None, 0), 1, off0).then_inc(T["up_done"], 1)
                        turn_z(Step(None, 1), False)
                        two_step_loop(pe, XS, step)

            comb = ExitStack()
            with comb:
                YG = sb("YG", [P, 2, NT, D], F32, comb)
                y_landed = [sem(f"y_landed{t}", comb) for t in range(NT)]
                first_added = sem("first_added", comb)
                ready = sem("ready", comb)
                out_done = sem("out_done", comb)
                yg_zero = sem("yg_zero", comb)

                with nc.Block() as block:
                    @block.gpsimd
                    def _(pool):
                        nc.gpsimd.memset(YG[:, :, NT - 1, :], 0.0).then_inc(yg_zero, 1)
                        pool.wait_ge(yg_zero, 1)
                        for t in range(NT):
                            for k in range(2):
                                nc.gpsimd.indirect_dma_start(
                                    out=YG[:, k, t, :], out_offset=None, in_=slots_out[:, :],
                                    in_offset=bass.IndirectOffsetOnAxis(ap=pos_i[:, k, t:t + 1], axis=0),
                                    bounds_check=XS * P - 1, oob_is_err=False).then_inc(y_landed[t], DMA)

                    @block.vector
                    def _(dve):
                        for t in range(NT):
                            dve.wait_ge(y_landed[t], 2 * DMA)
                            nc.vector.scalar_tensor_tensor(X[:, t, :], YG[:, 0, t, :], w_top[:, 0, t:t + 1],
                                                           X[:, t, :], ALU.mult, ALU.add).then_inc(first_added, 1)
                            dve.wait_ge(first_added, t + 1)
                            nc.vector.scalar_tensor_tensor(X[:, t, :], YG[:, 1, t, :], w_top[:, 1, t:t + 1],
                                                           X[:, t, :], ALU.mult, ALU.add).then_inc(ready, 1)

                    @block.sync
                    def _(sp):
                        for t in range(NT):
                            rows = P if t < NT - 1 else LAST
                            sp.wait_ge(ready, t + 1)
                            sp.dma_start(out[t * P:t * P + rows, :], X[0:rows, t, :]).then_inc(out_done, DMA)
                        sp.wait_ge(out_done, NT * DMA)


_INS = ['x', 'edges', 'edge_attr_64', 'L0_gnn_W', 'L0_gnn_W_e', 'L0_gnn_att_src', 'L0_gnn_att_dst',
        'L0_gnn_att_edge', 'L0_gnn_bias', 'L0_gnn_gamma', 'L0_gnn_beta', 'L0_ffn_Wg', 'L0_ffn_bg',
        'L0_ffn_W1', 'L0_ffn_b1', 'L0_ffn_W2', 'L0_ffn_b2']


def kernel(**inputs):
    import numpy as np
    import concourse.bacc as bacc
    from concourse.bass_utils import run_bass_kernel_spmd

    inputs["edges"] = np.stack([np.asarray(inputs["src"]), np.asarray(inputs["dst"])])
    nc = bacc.Bacc("TRN2", target_bir_lowering=False, num_devices=1)
    arrays, args = {}, []
    for name in _INS:
        a = np.ascontiguousarray(inputs[name])
        arrays[f"in_{name}"] = a
        args.append(nc.dram_tensor(f"in_{name}", a.shape, mybir.dt.from_np(a.dtype), kind="ExternalInput").ap())
    shape = arrays["in_x"].shape
    o = nc.dram_tensor("out_x", shape, F32, kind="ExternalOutput").ap()
    build(nc, *args, o)
    r = run_bass_kernel_spmd(nc, [arrays], core_ids=[0])
    return r.results[0]["out_x"]
```
